# Optimizing a Trainium2 kernel written in Bass

```python
import numpy as np
import jax
import jax.numpy as jnp

def _softmax(x, axis=-1):
    return jax.nn.softmax(x, axis=axis)

def _gelu(x):
    return jax.nn.gelu(x, approximate=True)

def _silu(x):
    return jax.nn.silu(x)

def _sigmoid(x):
    return jax.nn.sigmoid(x)

def _layernorm(x, axis=-1, eps=1e-05):
    m = jnp.mean(x, axis=axis, keepdims=True)
    v = jnp.var(x, axis=axis, keepdims=True)
    return (x - m) / jnp.sqrt(v + eps)

def _scatter_add(tgt, idx, src, axis=0):
    return tgt.at[idx].add(src)

def _segment_sum(src, seg, n):
    return jax.ops.segment_sum(src, seg, n)
kernel_name = 'mk_adj_resnorm_d1_adj_r2_e34f85'

def setup_inputs(seed: int=0):
    np.random.seed(seed)
    _w = jnp.asarray

    def _rec_inputs():
        import jax
        import jax.numpy as jnp
        _gk = jax.random.key(seed)
        x = 7.22e-05 + 1 * jax.random.normal(jax.random.fold_in(_gk, 1), (8, 1024, 256), jnp.float32)
        _a = jax.random.bernoulli(jax.random.fold_in(_gk, 2), 0.00390625, (1024, 1024))
        _a = jnp.logical_or(_a, jnp.swapaxes(_a, -1, -2))
        _a = jnp.logical_or(_a, jnp.eye(1024, dtype=bool))
        _af = _a.astype(jnp.float32)
        _af = _af * jax.random.uniform(jax.random.fold_in(_gk, 3), (1024, 1024), jnp.float32, 0.05, 0.00390622)
        adj = _af
        return (x, adj)
    x, adj = _rec_inputs()

    def _L0_gnn_setup():
        import jax, jax.numpy as jnp
        import numpy as np
        B, N, D, T = (64, 128, 256, 3)

        def _lin(v, W, b):
            return jnp.einsum('...i,oi->...o', v, W) + b
        key = jax.random.key(seed)
        ks = jax.random.split(key, 12)
        s2 = 1.0 / np.sqrt(2 * D)
        s1 = 1.0 / np.sqrt(D)
        return {'x': jax.random.normal(ks[0], (B, N, D), jnp.float32), 'in_mat': jax.random.uniform(ks[1], (N, N), jnp.float32) / N, 'out_mat': jax.random.uniform(ks[2], (N, N), jnp.float32) / N, 'w3_w': jax.random.normal(ks[3], (D, 2 * D), jnp.float32) * s2, 'w3_b': jnp.zeros((D,), jnp.float32), 'u3_w': jax.random.normal(ks[4], (D, D), jnp.float32) * s1, 'u3_b': jnp.zeros((D,), jnp.float32), 'w4_w': jax.random.normal(ks[5], (D, 2 * D), jnp.float32) * s2, 'w4_b': jnp.zeros((D,), jnp.float32), 'w5_w': jax.random.normal(ks[6], (D, 2 * D), jnp.float32) * s2, 'w5_b': jnp.zeros((D,), jnp.float32), 'u5_w': jax.random.normal(ks[7], (D, D), jnp.float32) * s1, 'u5_b': jnp.zeros((D,), jnp.float32)}
    _L0_gnn_all = _L0_gnn_setup()
    _L0_gnn_in = {k: v for k, v in _L0_gnn_all.items() if k in ('w3_w', 'w3_b', 'u3_w', 'u3_b', 'w4_w', 'w4_b', 'w5_w', 'w5_b', 'u5_w', 'u5_b')}
    del _L0_gnn_all
    return {'x': x, 'adj': adj, 'L0_gnn_w3_w': _L0_gnn_in['w3_w'], 'L0_gnn_w3_b': _L0_gnn_in['w3_b'], 'L0_gnn_u3_w': _L0_gnn_in['u3_w'], 'L0_gnn_u3_b': _L0_gnn_in['u3_b'], 'L0_gnn_w4_w': _L0_gnn_in['w4_w'], 'L0_gnn_w4_b': _L0_gnn_in['w4_b'], 'L0_gnn_w5_w': _L0_gnn_in['w5_w'], 'L0_gnn_w5_b': _L0_gnn_in['w5_b'], 'L0_gnn_u5_w': _L0_gnn_in['u5_w'], 'L0_gnn_u5_b': _L0_gnn_in['u5_b']}

def reference(x, adj, L0_gnn_w3_w, L0_gnn_w3_b, L0_gnn_u3_w, L0_gnn_u3_b, L0_gnn_w4_w, L0_gnn_w4_b, L0_gnn_w5_w, L0_gnn_w5_b, L0_gnn_u5_w, L0_gnn_u5_b):
    import jax
    import jax.numpy as jnp

    def _L0_gnn_ref(x, in_mat, out_mat, w3_w, w3_b, u3_w, u3_b, w4_w, w4_b, w5_w, w5_b, u5_w, u5_b):
        import jax, jax.numpy as jnp
        import numpy as np
        B, N, D, T = (64, 128, 256, 3)

        def _lin(v, W, b):
            return jnp.einsum('...i,oi->...o', v, W) + b
        h = x
        for _ in range(T):
            a_in = jnp.einsum('nm,bmd->bnd', in_mat, h)
            a_out = jnp.einsum('nm,bmd->bnd', out_mat, h)
            av = jnp.concatenate([a_in, a_out], axis=-1)
            z = jax.nn.sigmoid(_lin(av, w3_w, w3_b) + _lin(h, u3_w, u3_b))
            r = jax.nn.sigmoid(_lin(av, w4_w, w4_b) + _lin(h, u3_w, u3_b))
            hv = jnp.tanh(_lin(av, w5_w, w5_b) + _lin(r * h, u5_w, u5_b))
            h = (1.0 - z) * h + z * hv
        return h
    x = _layernorm(x + _L0_gnn_ref(x, adj, adj, L0_gnn_w3_w, L0_gnn_w3_b, L0_gnn_u3_w, L0_gnn_u3_b, L0_gnn_w4_w, L0_gnn_w4_b, L0_gnn_w5_w, L0_gnn_w5_b, L0_gnn_u5_w, L0_gnn_u5_b), axis=-1)
    return x

_drawn_inputs = setup_inputs


def setup_inputs(seed=0):
    import zlib

    import numpy as np

    out = dict(_drawn_inputs(seed))
    spreads = {'L0_gnn_w3_b': (0.0, 0.46),
     'L0_gnn_u3_b': (0.0, 0.407),
     'L0_gnn_w4_b': (0.0, 0.8),
     'L0_gnn_w5_b': (0.0, 0.1),
     'L0_gnn_u5_b': (0.0, 0.1)}
    factors = {'L0_gnn_w3_w': 2.983, 'L0_gnn_w4_w': 7.184}
    for name, (base, spread) in spreads.items():
        noise = np.random.default_rng([zlib.crc32(name.encode()), seed]).standard_normal(out[name].shape)
        drawn = base * np.exp(spread * noise) if base else spread * noise
        out[name] = jnp.asarray(drawn.astype(out[name].dtype))
    for name, factor in factors.items():
        out[name] = (out[name] * factor).astype(out[name].dtype)
    return out
```

```python
from contextlib import ExitStack

import concourse.bass as bass
from concourse import mybir

F32 = mybir.dt.float32
F32R = mybir.dt.float32r
ALU = mybir.AluOpType
ACT = mybir.ActivationFunctionType

P = 128
STEPS = 3
EPS = 1e-5
DMA = 16


def gnn_program(nc, x, adj, w3_w, w3_b, u3_w, u3_b, w4_w, w4_b, w5_w, w5_b, u5_w, u5_b, out):
    B, N, D = x.shape
    KT = N // P
    DT = D // P
    CH = 512
    CHUNKS = N // CH
    KC = KT // CHUNKS
    PAIRS = B // 2
    POS = 2 * STEPS
    assert CHUNKS == 2 and DT == 2 and B % 2 == 0 and N % CH == 0

    with ExitStack() as ctx:
        def sb(name, shape, dt=F32):
            return ctx.enter_context(nc.sbuf_tensor(name, shape, dt))

        def sem(name):
            return ctx.enter_context(nc.semaphore(name))

        ident = sb("ident", [P, P])
        adjT_hi = sb("adjT_hi", [P, KT, N], F32R)
        adjT_lo = sb("adjT_lo", [P, KT, N], F32R)
        W = ("u3", "w4", "w3", "w5", "u5")
        w_hi = {w: sb(f"{w}T_hi", [P, DT, D], F32R) for w in W}
        w_lo = {w: sb(f"{w}T_lo", [P, DT, D], F32R) for w in W}
        bias_row = sb("bias_row", [5 * DT, P])
        bias_in = sb("bias_in", [P, 5, DT])
        bias = sb("bias", [P, 3, DT])
        minus_half = sb("minus_half", [P, KT])
        hT = [sb(f"hT{i}", [P, DT, N]) for i in range(2)]
        hnat_hi = [sb(f"hnat_hi{i}", [P, KT, D], F32R) for i in range(2)]
        hnat_lo = [sb(f"hnat_lo{i}", [P, KT, D], F32R) for i in range(2)]
        x_in = sb("x_in", [P, KT, D])
        x_res = sb("x_res", [P, KT, D])
        stats = sb("stats", [P, KT, 6])
        mean = sb("mean", [P, KT])
        half_dev = sb("half_dev", [P, KT])
        sq_dev = sb("sq_dev", [P, KT])
        sum_sq = sb("sum_sq", [P, KT])
        var_eps = sb("var_eps", [P, KT])
        rstd = sb("rstd", [P, KT])
        agg_hi = [sb(f"agg_hi{c}", [P, DT, CH], F32R) for c in range(2)]
        agg_lo = [sb(f"agg_lo{c}", [P, DT, CH], F32R) for c in range(2)]
        mov_hi = [sb(f"mov_hi{c}", [P, DT, CH], F32R) for c in range(2)]
        mov_lo = [sb(f"mov_lo{c}", [P, DT, CH], F32R) for c in range(2)]
        zbuf = [sb(f"zbuf{c}", [P, DT, CH]) for c in range(2)]
        rbuf = [sb(f"rbuf{c}", [P, DT, CH]) for c in range(2)]

        slot = [ctx.enter_context(nc.psum_tensor(f"slot{i}", [P, DT, CH], F32)) for i in range(4)]

        stage4 = [zbuf[0], zbuf[1], rbuf[0], rbuf[1]]
        adj_row = [t[:].rearrange("p a n -> p (a n)") for t in stage4]
        adj_row += [t[:].rearrange("p a n -> p (a n)")[:, i * N:(i + 1) * N] for t in (x_res, hT[1]) for i in range(2)]
        w_row = {w: stage4[i] for i, w in enumerate(("w3", "w4", "w5"))}
        w_row["u3"] = rbuf[1][:, 0, :].rearrange("p (a i) -> p a i", a=DT)
        w_row["u5"] = rbuf[1][:, 1, :].rearrange("p (a i) -> p a i", a=DT)

        s_adj = [sem(f"adj_row_loaded{j}") for j in range(KT)]
        s_w = sem("weights_loaded")
        s_b = sem("biases_loaded")
        s_xin = sem("x_in_loaded")
        s_xres = sem("x_res_loaded")
        s_stored = sem("stored")
        s_ident0 = sem("ident_zeroed")
        s_ident = sem("ident_ready")
        s_half = sem("minus_half_ready")
        s_adjT = sem("adj_transposed")
        s_adj_hi = sem("adj_hi_ready")
        s_adj_lo = sem("adj_lo_ready")
        s_wsum = sem("weight_halves_added")
        s_wT = sem("weights_transposed")
        s_w_hi = sem("weights_hi_ready")
        s_w_lo = sem("weights_lo_ready")
        s_bias_in = sem("bias_transposed")
        s_bias = sem("bias_ready")
        s_A = sem("A_done")
        s_S = sem("S_done")
        s_R = sem("R_done")
        s_Z = sem("Z_done")
        s_V = sem("V_done")
        s_T = sem("transposed")
        s_F = sem("final_transposed")
        s_xT = sem("xT_copied")
        s_nat_hi = sem("nat_hi_ready")
        s_h_hi = sem("h_hi_ready")
        s_agg_hi = sem("agg_hi_ready")
        s_S_cp = sem("S_copied")
        s_r = sem("r_ready")
        s_rh_hi = sem("rh_hi_ready")
        s_z = sem("z_ready")
        s_cand = sem("candidate_ready")
        s_nat_lo = sem("nat_lo_ready")
        s_h_lo = sem("h_lo_ready")
        s_agg_lo = sem("agg_lo_ready")
        s_r_sum = sem("r_summed")
        s_rh = sem("rh_ready")
        s_rh_lo = sem("rh_lo_ready")
        s_z_sum = sem("z_summed")
        s_diff = sem("candidate_minus_h")
        s_step = sem("z_times_difference")
        s_h = sem("h_updated")
        s_res = sem("residual_added")
        s_stat = sem("stats_ready")
        s_mom = sem("halves_combined")
        s_mean = sem("mean_ready")
        s_sq = sem("sq_dev_ready")
        s_var0 = sem("var_ready")
        s_var = sem("var_eps_ready")
        s_rstd = sem("rstd_ready")
        s_out = sem("out_ready")

        def chunk(t, c):
            return t[:, :, c * CH:(c + 1) * CH]

        def ktiles(t, c):
            return t[:, c * KC:(c + 1) * KC, :]

        def flat(ps):
            return ps[:].rearrange("p a (k d) -> p (a k) d", d=D)

        def f32(ap):
            return ap.bitcast(F32)

        def nth(g, c):
            return 2 * g + c + 1

        def turns(eng, turn):
            turn(0, 0, first=True)
            with eng.Fori(0, PAIRS - 1) as p:
                for pos in range(1, POS):
                    turn(p, pos)
                turn(p + 1, 0)
            for pos in range(1, POS):
                turn(PAIRS - 1, pos, last=True)

        block = ctx.enter_context(nc.Block())

        @block.sync
        def _(sp):
            def nat(t, n):
                return t[n:n + 1, :, :].rearrange("b (k p) d -> p (b k) d", p=P) if isinstance(n, int) else \
                    t[bass.ds(n, 1), :, :].rearrange("b (k p) d -> p (b k) d", p=P)

            def load_adj(j):
                sp.dma_start(adj_row[j], adj[j * P:(j + 1) * P, :]).then_inc(s_adj[j], DMA)

            for j in range(KC):
                load_adj(j)
            sp.dma_start(x_in[:], nat(x, 0)).then_inc(s_xin, DMA)
            for j in range(KC, KT):
                load_adj(j)
            for i, (w, src) in enumerate((("w3", w3_w), ("w4", w4_w), ("w5", w5_w))):
                sp.wait_ge(s_adjT, i + 1)
                sp.dma_start(w_row[w][:], src.rearrange("(a p) i -> p a i", p=P)).then_inc(s_w, DMA)
            sp.wait_ge(s_adjT, KC)
            for w, src in (("u3", u3_w), ("u5", u5_w)):
                sp.dma_start(w_row[w], src.rearrange("(a p) i -> p a i", p=P)).then_inc(s_w, DMA)

            def free_x_in(g):
                sp.wait_ge(s_T, nth(g, 1))
                sp.wait_ge(s_nat_lo, nth(g, 1))

            def store(n):
                sp.wait_ge(s_out, n + 1)
                sp.dma_start(nat(out, n), x_res[:]).then_inc(s_stored, DMA)

            free_x_in(0)
            sp.dma_start(x_in[:], nat(x, 1)).then_inc(s_xin, DMA)
            sp.wait_ge(s_adjT, KT)
            sp.dma_start(x_res[:], nat(x, 0)).then_inc(s_xres, DMA)
            with sp.Fori(0, PAIRS - 1) as p:
                free_x_in(POS * p + 1)
                sp.dma_start(x_in[:], nat(x, 2 * p + 2)).then_inc(s_xin, DMA)
                store(2 * p)
                sp.wait_ge(s_stored, DMA * (2 * p + 1))
                sp.dma_start(x_res[:], nat(x, 2 * p + 1)).then_inc(s_xres, DMA)
                free_x_in(POS * p + POS)
                sp.dma_start(x_in[:], nat(x, 2 * p + 3)).then_inc(s_xin, DMA)
                store(2 * p + 1)
                sp.wait_ge(s_stored, DMA * (2 * p + 2))
                sp.dma_start(x_res[:], nat(x, 2 * p + 2)).then_inc(s_xres, DMA)
            store(B - 2)
            sp.wait_ge(s_out, B)
            sp.dma_start(nat(out, B - 1), x_in[:]).then_inc(s_stored, DMA)
            sp.wait_ge(s_stored, DMA * B)

        @block.gpsimd
        def _(pool):
            nc.gpsimd.memset(ident[:], 0.0).then_inc(s_ident0, 1)
            nc.gpsimd.memset(minus_half[:], -0.5).then_inc(s_half, 1)
            pool.wait_ge(s_ident0, 1)
            nc.gpsimd.affine_select(out=ident[:], in_=ident[:], compare_op=ALU.not_equal, fill=1.0, base=0,
                                    pattern=[[-1, P]], channel_multiplier=1).then_inc(s_ident, 1)
            for i, b in enumerate((w3_b, u3_b, w4_b, w5_b, u5_b)):
                pool.dma_start(bias_row[i * DT:(i + 1) * DT, :], b.rearrange("(a p) -> a p", p=P)).then_inc(s_b, DMA)
            pool.wait_ge(s_half, 1)
            with pool.Fori(0, B) as n:
                pool.wait_ge(s_var, n + 1)
                nc.gpsimd.tensor_tensor(rstd[:], var_eps[:], minus_half[:], ALU.pow).then_inc(s_rstd, 1)

        @block.tensor
        def _(pe):
            def product(ps, terms):
                for a in range(DT):
                    todo = [(s[:, k, a * P:(a + 1) * P], m) for stat, mov in terms for k, (mh, ml) in enumerate(mov)
                            for s, m in ((stat[0], mh), (stat[1], mh), (stat[0], ml))]
                    for i, (s, m) in enumerate(todo):
                        last = nc.tensor.matmul(ps[:, a, :], s, m, start=(i == 0), stop=(i == len(todo) - 1))
                return last

            def halves(hi, lo):
                return [(hi[:, k, :], lo[:, k, :]) for k in range(DT)]

            def gate(ps, w, hi, lo):
                return product(ps, [((w_hi[w], w_lo[w]), halves(hi, lo))])

            def turn_blocks(ps, src):
                for k in range(KC):
                    for a in range(DT):
                        last = src(ps, k, a)
                return last

            def to_nat(i, c):
                def block_(ps, k, a):
                    at = (c * KC + k) * P
                    return nc.tensor.transpose(flat(ps)[:, k, a * P:(a + 1) * P], hT[i][:, a, at:at + P], ident[:])
                return block_

            def to_T(c):
                def block_(ps, k, a):
                    return nc.tensor.transpose(ps[:, a, k * P:(k + 1) * P],
                                               x_in[:, c * KC + k, a * P:(a + 1) * P], ident[:])
                return block_

            def adj_turn(j, s):
                pe.wait_ge(s_adj[j], DMA)
                for k in range(KT):
                    last = nc.tensor.transpose(slot[s][:].rearrange("p a n -> p (a n)")[:, k * P:(k + 1) * P],
                                               adj_row[j][:, k * P:(k + 1) * P], ident[:])
                last.then_inc(s_adjT, 1)

            def weight_turn(s, ws):
                for i, w in enumerate(ws):
                    for it in range(DT):
                        for ot in range(DT):
                            last = nc.tensor.transpose(slot[s][:, i, it * D + ot * P:it * D + (ot + 1) * P],
                                                       w_row[w][:, ot, it * P:(it + 1) * P], ident[:])
                last.then_inc(s_wT, 1)

            pe.wait_ge(s_ident, 1)
            for j in range(KC):
                adj_turn(j, j)
            pe.wait_ge(s_xin, DMA)
            for c in range(CHUNKS):
                pe.wait_ge(s_adj_lo, c + 1)
                turn_blocks(slot[c], to_T(c)).then_inc(s_T, 1)
            for j, s in zip(range(KC, KT), (2, 3, 0, 1)):
                if s in (2, 3):
                    pe.wait_ge(s_adj_lo, s + 1)
                else:
                    pe.wait_ge(s_xT, s + 1)
                adj_turn(j, s)

            def weights_first():
                pe.wait_ge(s_w, 5 * DMA)
                pe.wait_ge(s_wsum, 3)
                pe.wait_ge(s_adj_lo, KC + 2)
                weight_turn(2, ("u3", "w4"))
                weight_turn(3, ("w3", "w5"))

            def weights_last():
                pe.wait_ge(s_w_lo, 1)
                pe.wait_ge(s_b, 5 * DMA)
                nc.tensor.transpose(slot[2][:, 1, 0:5 * DT], bias_row[:], ident[0:5 * DT, 0:5 * DT])
                weight_turn(2, ("u5",))

            def turn(p, pos, first=False, last=False):
                g = POS * p + pos
                i = pos % 2
                final = (pos == 0 and not first) or pos == POS - 1
                prepare = not (last and pos == POS - 1)
                fresh = pos in (0, POS - 1)
                for c in range(CHUNKS):
                    if c == 0:
                        pe.wait_ge(s_nat_lo, nth(g, 1))
                    if first:
                        pe.wait_ge(s_adj_lo, KT)
                    elif pos in (0, 1):
                        pe.wait_ge(s_xT, nth(2 * p + pos, c))
                    product(slot[c], [((hnat_hi[i], hnat_lo[i]),
                                       [(chunk(adjT_hi, c)[:, k, :], chunk(adjT_lo, c)[:, k, :])
                                        for k in range(KT)])]).then_inc(s_A, 1)
                    if first:
                        (weights_first if c == 0 else weights_last)()
                for c in range(CHUNKS):
                    pe.wait_ge(s_h_lo, nth(g, c))
                    if first and c == 0:
                        pe.wait_ge(s_w_lo, 3)
                        pe.wait_ge(s_bias_in, 1)
                    elif c == 0:
                        pe.wait_ge(s_cand, nth(g - 1, 0))
                    else:
                        pe.wait_ge(s_agg_lo, nth(g, 1))
                    gate(slot[2 - c], "u3", mov_hi[c], mov_lo[c]).then_inc(s_S, 1)
                    pe.wait_ge(s_agg_lo, nth(g, c))
                    if c == 1:
                        pe.wait_ge(s_S_cp, nth(g, 0))
                    elif not first:
                        pe.wait_ge(s_cand, nth(g - 1, 1))
                    gate(slot[3 - c], "w4", agg_hi[c], agg_lo[c]).then_inc(s_R, 1)
                    if c == 1:
                        pe.wait_ge(s_r_sum, nth(g, 0))
                    gate(slot[3 * c], "w3", agg_hi[c], agg_lo[c]).then_inc(s_Z, 1)

                def prepare_next():
                    if fresh:
                        pe.wait_ge(s_xin, DMA * (2 * p + 2 if pos == 0 else 2 * p + 3))
                    for c in range(CHUNKS):
                        if final:
                            pe.wait_ge(s_res, nth(2 * p + (-1 if pos == 0 else 0), c))
                        elif c == 0:
                            pe.wait_ge(s_z_sum, nth(g, 0))
                        else:
                            pe.wait_ge(s_S_cp, nth(g, 1))
                        if not fresh:
                            pe.wait_ge(s_h, nth(g - 1, c))
                        turn_blocks(slot[c], to_T(c) if fresh else to_nat(1 - i, c)).then_inc(s_T, 1)

                def finish_other():
                    for c in range(CHUNKS):
                        pe.wait_ge(s_h, nth(g - 1, c))
                        if c == 0:
                            pe.wait_ge(s_z_sum, nth(g, 0))
                        else:
                            pe.wait_ge(s_S_cp, nth(g, 1))
                        turn_blocks(slot[c], to_nat(1 - i, c)).then_inc(s_F, 1)

                if final:
                    finish_other()
                else:
                    prepare_next()
                for c in range(CHUNKS):
                    pe.wait_ge(s_rh_lo, nth(g, c))
                    pe.wait_ge((s_r_sum, s_z_sum)[c], nth(g, 1))
                    product(slot[2 + c], [((w_hi["w5"], w_lo["w5"]), halves(agg_hi[c], agg_lo[c])),
                                          ((w_hi["u5"], w_lo["u5"]), halves(mov_hi[c], mov_lo[c]))]).then_inc(s_V, 1)
                    if c == 0 and final and prepare:
                        prepare_next()

            turns(pe, turn)
            for c in range(CHUNKS):
                pe.wait_ge(s_res, nth(B - 2, c))
                pe.wait_ge(s_h, nth(POS * PAIRS - 1, c))
                turn_blocks(slot[c], to_nat(1, c)).then_inc(s_F, 1)

        @block.scalar
        def _(act):
            def copy(dst, src):
                return nc.scalar.activation(dst, src, ACT.Copy)

            def adj_hi(j, s):
                act.wait_ge(s_adjT, j + 1)
                copy(adjT_hi[:, :, j * P:(j + 1) * P],
                     slot[s][:].rearrange("p a (k n) -> p (a k) n", n=P)).then_inc(s_adj_hi, 1)

            for j in range(KC):
                adj_hi(j, j)
            act.wait_ge(s_xin, DMA)
            for c in range(CHUNKS):
                copy(ktiles(hnat_hi[0], c), ktiles(x_in, c)).then_inc(s_nat_hi, 1)
            for c in range(CHUNKS):
                act.wait_ge(s_T, c + 1)
                copy(chunk(hT[0], c), slot[c][:]).then_inc(s_xT, 1)
            for j, s in zip(range(KC, KT), (2, 3, 0, 1)):
                adj_hi(j, s)

            def weight_hi(s, n, ws):
                act.wait_ge(s_wT, n)
                for k, w in enumerate(ws):
                    last = copy(w_hi[w][:].rearrange("p a o -> p (a o)"), slot[s][:, k, :])
                last.then_inc(s_w_hi, 1)

            def turn(p, pos, first=False, last=False):
                g = POS * p + pos
                i = pos % 2
                final = (pos == 0 and not first) or pos == POS - 1
                prepare = not (last and pos == POS - 1)
                fresh = pos in (0, POS - 1)
                for c in range(CHUNKS):
                    act.wait_ge(s_A, nth(g, c))
                    if not first:
                        act.wait_ge(s_V, nth(g - 1, c))
                    copy(agg_hi[c][:], slot[c][:]).then_inc(s_agg_hi, 1)
                    if first and c == 0:
                        weight_hi(2, 1, ("u3", "w4"))
                        weight_hi(3, 2, ("w3", "w5"))
                if first:
                    weight_hi(2, 3, ("u5",))
                    copy(bias_in[:].rearrange("p b a -> p (b a)"), slot[2][:, 1, 0:5 * DT]).then_inc(s_bias_in, 1)
                    act.wait_ge(s_bias, 3)
                for c in range(CHUNKS):
                    act.wait_ge(s_S, nth(g, c))
                    if not first:
                        act.wait_ge(s_step, nth(g - 1, c))
                    copy(zbuf[c][:], slot[2 - c][:]).then_inc(s_S_cp, 1)
                    act.wait_ge(s_r_sum, nth(g, c))
                    for a in range(DT):
                        r = nc.scalar.activation(rbuf[c][:, a, :], rbuf[c][:, a, :], ACT.Sigmoid,
                                                 bias=bias[:, 1, a:a + 1])
                    r.then_inc(s_r, 1)
                    act.wait_ge(s_rh, nth(g, c))
                    copy(mov_hi[c][:], rbuf[c][:]).then_inc(s_rh_hi, 1)
                    act.wait_ge(s_z_sum, nth(g, c))
                    for a in range(DT):
                        z = nc.scalar.activation(zbuf[c][:, a, :], zbuf[c][:, a, :], ACT.Sigmoid,
                                                 bias=bias[:, 0, a:a + 1])
                    z.then_inc(s_z, 1)

                def prepare_next():
                    for c in range(CHUNKS):
                        act.wait_ge(s_T, nth(g + 1, c))
                        if fresh:
                            copy(chunk(hT[1 - i], c), slot[c][:]).then_inc(s_xT, 1)
                        else:
                            copy(ktiles(hnat_hi[1 - i], c), flat(slot[c])).then_inc(s_nat_hi, 1)

                if fresh and prepare:
                    act.wait_ge(s_xin, DMA * (2 * p + 2 if pos == 0 else 2 * p + 3))
                    if not first:
                        act.wait_ge(s_A, nth(g - 1, 1))
                    for c in range(CHUNKS):
                        copy(ktiles(hnat_hi[1 - i], c), ktiles(x_in, c)).then_inc(s_nat_hi, 1)
                if not final:
                    prepare_next()
                for c in range(CHUNKS):
                    act.wait_ge(s_V, nth(g, c))
                    for a in range(DT):
                        v = nc.scalar.activation(rbuf[c][:, a, :], slot[2 + c][:, a, :], ACT.Tanh,
                                                 bias=bias[:, 2, a:a + 1])
                    v.then_inc(s_cand, 1)
                    if c == 0 and final and prepare:
                        prepare_next()

            turns(act, turn)

        @block.vector
        def _(dve):
            def lo(dst, src, hi):
                return nc.vector.tensor_tensor(dst, src, f32(hi), ALU.subtract)

            def adj_lo(j, s):
                dve.wait_ge(s_adj_hi, j + 1)
                at = adjT_hi[:, :, j * P:(j + 1) * P]
                lo(adjT_lo[:, :, j * P:(j + 1) * P],
                   slot[s][:].rearrange("p a (k n) -> p (a k) n", n=P), at).then_inc(s_adj_lo, 1)

            def split_x(i, g):
                for c in range(CHUNKS):
                    dve.wait_ge(s_nat_hi, nth(g, c))
                    lo(ktiles(hnat_lo[i], c), ktiles(x_in, c), ktiles(hnat_hi[i], c)).then_inc(s_nat_lo, 1)

            for j in range(KC):
                adj_lo(j, j)
            split_x(0, 0)
            for j, s in zip(range(KC, KT), (2, 3, 0, 1)):
                adj_lo(j, s)
            dve.wait_ge(s_w, 5 * DMA)
            for w in ("w3", "w4", "w5"):
                nc.vector.tensor_tensor(w_row[w][:, :, 0:D], w_row[w][:, :, 0:D], w_row[w][:, :, D:2 * D],
                                        ALU.add).then_inc(s_wsum, 1)

            def weight_lo(s, n, ws):
                dve.wait_ge(s_w_hi, n)
                for k, w in enumerate(ws):
                    last = lo(w_lo[w][:].rearrange("p a o -> p (a o)"), slot[s][:, k, :],
                              w_hi[w][:].rearrange("p a o -> p (a o)"))
                last.then_inc(s_w_lo, 1)

            def update(g, i, c):
                h = chunk(hT[i], c)
                dve.wait_ge(s_cand, nth(g, c))
                nc.vector.tensor_tensor(rbuf[c][:], rbuf[c][:], h, ALU.subtract).then_inc(s_diff, 1)
                dve.wait_ge(s_z, nth(g, c))
                dve.wait_ge(s_diff, nth(g, c))
                nc.vector.tensor_tensor(rbuf[c][:], rbuf[c][:], zbuf[c][:], ALU.mult).then_inc(s_step, 1)
                dve.wait_ge(s_step, nth(g, c))
                nc.vector.tensor_tensor(h, h, rbuf[c][:], ALU.add).then_inc(s_h, 1)

            def residual(n, t):
                for c in range(CHUNKS):
                    dve.wait_ge(s_F, nth(n, c))
                    nc.vector.tensor_tensor(ktiles(t, c), ktiles(t, c), flat(slot[c]), ALU.add).then_inc(s_res, 1)

            def layernorm(n, t):
                dve.wait_ge(s_res, nth(n, 1))
                for k in range(KT):
                    nc.vector.bn_stats(stats[:, k, :], t[:, k, :]).then_inc(s_stat, 1)
                dve.wait_ge(s_stat, KT * n + KT)
                nc.vector.tensor_tensor(mean[:], stats[:, :, 1], stats[:, :, 4], ALU.add).then_inc(s_mom, 1)
                nc.vector.tensor_tensor(half_dev[:], stats[:, :, 1], stats[:, :, 4], ALU.subtract).then_inc(s_mom, 1)
                nc.vector.tensor_tensor(sum_sq[:], stats[:, :, 2], stats[:, :, 5], ALU.add).then_inc(s_mom, 1)
                dve.wait_ge(s_mom, 3 * n + 3)
                nc.vector.tensor_scalar(mean[:], mean[:], 0.5, None, ALU.mult).then_inc(s_mean, 1)
                nc.vector.scalar_tensor_tensor(sq_dev[:], half_dev[:], 0.25, half_dev[:], ALU.mult,
                                               ALU.mult).then_inc(s_sq, 1)
                dve.wait_ge(s_sq, n + 1)
                nc.vector.scalar_tensor_tensor(var_eps[:], sum_sq[:], 1.0 / D, sq_dev[:], ALU.mult,
                                               ALU.add).then_inc(s_var0, 1)
                dve.wait_ge(s_var0, n + 1)
                nc.vector.tensor_scalar(var_eps[:], var_eps[:], EPS, None, ALU.add).then_inc(s_var, 1)
                dve.wait_ge(s_mean, n + 1)
                dve.wait_ge(s_rstd, n + 1)
                for k in range(KT):
                    last = nc.vector.tensor_scalar(t[:, k, :], t[:, k, :], mean[:, k:k + 1], rstd[:, k:k + 1],
                                                   ALU.subtract, ALU.mult)
                last.then_inc(s_out, 1)

            def turn(p, pos, first=False, last=False):
                g = POS * p + pos
                i = pos % 2
                final = (pos == 0 and not first) or pos == POS - 1
                prepare = not (last and pos == POS - 1)
                fresh = pos in (0, POS - 1)
                if not first:
                    update(g - 1, 1 - i, 1)
                for c in range(CHUNKS):
                    h = chunk(hT[i], c)
                    if pos in (0, 1):
                        dve.wait_ge(s_xT, nth(2 * p + pos, c))
                    else:
                        dve.wait_ge(s_h, nth(g - 2, c))
                    if not first:
                        dve.wait_ge(s_V, nth(g - 1, c))
                    nc.vector.tensor_copy(mov_hi[c][:], h).then_inc(s_h_hi, 1)
                    dve.wait_ge(s_h_hi, nth(g, c))
                    lo(mov_lo[c][:], h, mov_hi[c][:]).then_inc(s_h_lo, 1)
                for c in range(CHUNKS):
                    dve.wait_ge(s_agg_hi, nth(g, c))
                    lo(agg_lo[c][:], slot[c][:], agg_hi[c][:]).then_inc(s_agg_lo, 1)
                    if first and c == 0:
                        weight_lo(2, 1, ("u3", "w4"))
                        weight_lo(3, 2, ("w3", "w5"))
                if first:
                    weight_lo(2, 3, ("u5",))
                    dve.wait_ge(s_bias_in, 1)
                    for k, (a, b) in enumerate(((0, 1), (2, 1), (3, 4))):
                        nc.vector.tensor_tensor(bias[:, k, :], bias_in[:, a, :], bias_in[:, b, :],
                                                ALU.add).then_inc(s_bias, 1)
                for c in range(CHUNKS):
                    dve.wait_ge(s_R, nth(g, c))
                    dve.wait_ge(s_S_cp, nth(g, c))
                    nc.vector.tensor_tensor(rbuf[c][:], slot[3 - c][:], zbuf[c][:], ALU.add).then_inc(s_r_sum, 1)
                    dve.wait_ge(s_r, nth(g, c))
                    nc.vector.tensor_tensor(rbuf[c][:], rbuf[c][:], chunk(hT[i], c), ALU.mult).then_inc(s_rh, 1)
                    dve.wait_ge(s_Z, nth(g, c))
                    nc.vector.tensor_tensor(zbuf[c][:], slot[3 * c][:], zbuf[c][:], ALU.add).then_inc(s_z_sum, 1)
                    dve.wait_ge(s_rh_hi, nth(g, c))
                    lo(mov_lo[c][:], rbuf[c][:], mov_hi[c][:]).then_inc(s_rh_lo, 1)
                if fresh and prepare:
                    split_x(1 - i, g + 1)
                if final:
                    n = 2 * p - 1 if pos == 0 else 2 * p
                    dve.wait_ge(s_xres, DMA * (n + 1))
                    residual(n, x_res)
                elif not fresh:
                    for c in range(CHUNKS):
                        dve.wait_ge(s_nat_hi, nth(g + 1, c))
                        lo(ktiles(hnat_lo[1 - i], c), flat(slot[c]),
                           ktiles(hnat_hi[1 - i], c)).then_inc(s_nat_lo, 1)
                update(g, i, 0)
                if final:
                    layernorm(n, x_res)

            turns(dve, turn)
            update(POS * PAIRS - 1, 1, 1)
            residual(B - 1, x_in)
            layernorm(B - 1, x_in)


_INS = ["x", "adj"] + [f"L0_gnn_{n}" for n in ("w3_w", "w3_b", "u3_w", "u3_b", "w4_w", "w4_b", "w5_w", "w5_b", "u5_w", "u5_b")]


def kernel(**inputs):
    import numpy as _np
    import concourse.bacc as _bacc
    from concourse.bass_utils import run_bass_kernel_spmd as _run

    nc = _bacc.Bacc("TRN2", target_bir_lowering=False, num_devices=1)
    arrays, args = {}, []
    for name in _INS:
        a = _np.ascontiguousarray(inputs[name])
        arrays[f"in_{name}_dram"] = a
        args.append(nc.dram_tensor(f"in_{name}_dram", a.shape, mybir.dt.from_np(a.dtype), kind="ExternalInput").ap())
    args.append(nc.dram_tensor("out_dram", inputs["x"].shape, F32, kind="ExternalOutput").ap())
    gnn_program(nc, *args)
    return _run(nc, [arrays], core_ids=[0]).results[0]["out_dram"]
```

```python
from contextlib import ExitStack

import concourse.bass as bass
from concourse import mybir

F32 = mybir.dt.float32
F32R = mybir.dt.float32r
ALU = mybir.AluOpType
ACT = mybir.ActivationFunctionType

P = 128
STEPS = 3
EPS = 1e-5
DMA = 16
EXCHANGE = 16 * DMA


def gnn_program(nc, x, adj, w3_w, w3_b, u3_w, u3_b, w4_w, w4_b, w5_w, w5_b, u5_w, u5_b, out):
    B, N, D = x.shape
    Q, SQ = 4, 32
    KT = N // P
    DT = D // P
    CH = 512
    CHUNKS = N // CH
    TAIL = CH // P
    KC = KT // 2
    PAIRS = B // 2
    POS = 2 * STEPS
    assert CHUNKS == 2 and DT == 2 and B % 2 == 0 and N % CH == 0

    with ExitStack() as ctx:
        def sb(name, shape, dt=F32):
            return ctx.enter_context(nc.sbuf_tensor(name, shape, dt))

        def sem(name):
            return ctx.enter_context(nc.semaphore(name))

        ident = sb("ident", [P, P])
        adjT_hi = sb("adjT_hi", [P, KT, N], F32R)
        adjT_lo = sb("adjT_lo", [P, KT, N], F32R)
        W = ("u3", "w4", "w3", "w5", "u5")
        w_hi = {w: sb(f"{w}T_hi", [P, DT, D], F32R) for w in W}
        w_lo = {w: sb(f"{w}T_lo", [P, DT, D], F32R) for w in W}
        bias_row = sb("bias_row", [5 * DT, P])
        bias_in = sb("bias_in", [P, 5, DT])
        bias = sb("bias", [P, 3, DT])
        minus_half = sb("minus_half", [P, KT])
        hT = [sb(f"hT{i}", [P, Q, DT, N // Q]) for i in range(2)]
        hnat_hi = sb("hnat_hi", [P, KT, D], F32R)
        hnat_lo = sb("hnat_lo", [P, KT, D], F32R)
        blocks = sb("blocks", [P, Q, DT * KT * SQ])
        h_nodes = sb("h_nodes", [P, Q, DT, KT, SQ])
        x_in = sb("x_in", [P, KT, D])
        x_res = sb("x_res", [P, KT, D])
        stats = sb("stats", [P, KT, 6])
        mean2 = sb("mean2", [P, KT])
        minus_mean = sb("minus_mean", [P, KT])
        shift = sb("shift", [P, KT])
        dev = sb("dev", [P, KT])
        sq_dev = sb("sq_dev", [P, KT])
        sum_sq = sb("sum_sq", [P, KT])
        var_eps = sb("var_eps", [P, KT])
        rstd = sb("rstd", [P, KT])
        agg_hi = [sb(f"agg_hi{c}", [P, DT, CH], F32R) for c in range(2)]
        agg_lo = [sb(f"agg_lo{c}", [P, DT, CH], F32R) for c in range(2)]
        mov_hi = [sb(f"mov_hi{c}", [P, DT, CH], F32R) for c in range(2)]
        mov_lo = [sb(f"mov_lo{c}", [P, DT, CH], F32R) for c in range(2)]
        zbuf = [sb(f"zbuf{c}", [P, DT, CH]) for c in range(2)]
        rbuf = [sb(f"rbuf{c}", [P, DT, CH]) for c in range(2)]

        slot = [ctx.enter_context(nc.psum_tensor(f"slot{i}", [P, DT, CH], F32)) for i in range(4)]

        stage4 = [zbuf[0], zbuf[1], rbuf[0], rbuf[1]]
        adj_row = [t[:].rearrange("p a n -> p (a n)") for t in stage4]
        adj_row += [t[:, i * N:(i + 1) * N] for t in (x_res[:].rearrange("p k d -> p (k d)"),
                                                      h_nodes[:].rearrange("p i a k d -> p (i a k d)"))
                    for i in range(2)]
        w_row = {w: stage4[i] for i, w in enumerate(("w3", "w4", "w5"))}
        w_row["u3"] = rbuf[1][:, 0, :].rearrange("p (a i) -> p a i", a=DT)
        w_row["u5"] = rbuf[1][:, 1, :].rearrange("p (a i) -> p a i", a=DT)

        s_adj = [sem(f"adj_row_loaded{j}") for j in range(KT)]
        s_w = sem("weights_loaded")
        s_b = sem("biases_loaded")
        s_xin = sem("x_in_loaded")
        s_xres = sem("x_res_loaded")
        s_stored = sem("stored")
        s_ident0 = sem("ident_zeroed")
        s_ident = sem("ident_ready")
        s_half = sem("minus_half_ready")
        s_adjT = sem("adj_transposed")
        s_adj_hi = sem("adj_hi_ready")
        s_adj_lo = sem("adj_lo_ready")
        s_wsum = sem("weight_halves_added")
        s_wT = sem("weights_transposed")
        s_w_hi = sem("weights_hi_ready")
        s_w_lo = sem("weights_lo_ready")
        s_bias_in = sem("bias_transposed")
        s_bias = sem("bias_ready")
        s_tail = sem("last_batch_transposed")
        s_A = sem("A_done")
        s_S = sem("S_done")
        s_R = sem("R_done")
        s_Z = sem("Z_done")
        s_V = sem("V_done")
        s_prep = sem("exchanged")
        s_fin = sem("final_exchanged")
        s_nat_hi = sem("nat_hi_ready")
        s_h_hi = sem("h_hi_ready")
        s_agg_hi = sem("agg_hi_ready")
        s_S_cp = sem("S_copied")
        s_r = sem("r_ready")
        s_rh_hi = sem("rh_hi_ready")
        s_z = sem("z_ready")
        s_cand = sem("candidate_ready")
        s_blocks = sem("blocks_transposed")
        s_fblocks = sem("final_blocks_transposed")
        s_nat_lo = sem("nat_lo_ready")
        s_h_lo = sem("h_lo_ready")
        s_agg_lo = sem("agg_lo_ready")
        s_r_sum = sem("r_summed")
        s_rh = sem("rh_ready")
        s_rh_lo = sem("rh_lo_ready")
        s_z_sum = sem("z_summed")
        s_diff = sem("candidate_minus_h")
        s_step = sem("z_times_difference")
        s_h = sem("h_updated")
        s_res = sem("residual_added")
        s_stat = sem("stats_ready")
        s_halves = sem("halves_combined")
        s_mean = sem("mean_ready")
        s_sq = sem("sq_dev_ready")
        s_var0 = sem("var_ready")
        s_var = sem("var_eps_ready")
        s_rstd = sem("rstd_ready")
        s_shift = sem("shift_ready")
        s_out = sem("out_ready")

        def chunk(i, c):
            return hT[i][:, 2 * c:2 * c + 2, :, :].rearrange("p r a n -> p a r n")

        def like_h(t):
            return t[:].rearrange("p a (r n) -> p a r n", r=2)

        def features(t, a):
            return t[:, :, a * P:(a + 1) * P].rearrange("p k (i d) -> p k i d", i=Q)

        def exchanged(a):
            return h_nodes[:, :, a, :, :].rearrange("p i k d -> p k i d")

        def wide(ps):
            return ps[:].rearrange("p a n -> p (a n)")

        def adj_slot(j):
            return slot[j] if j < 4 else slot[2 + j % 2]

        def adj_columns(t, j):
            return (t[:].rearrange("p k (r j q) -> p k r j q", r=Q, j=KT)[:, :, :, j, :],
                    wide(adj_slot(j)).rearrange("p (k r q) -> p k r q", r=Q, q=SQ))

        def nth(g, c):
            return 2 * g + c + 1

        def turns(eng, turn):
            turn(0, 0, first=True)
            with eng.Fori(0, PAIRS - 1) as p:
                for pos in range(1, POS):
                    turn(p, pos)
                turn(p + 1, 0)
            for pos in range(1, POS):
                turn(PAIRS - 1, pos, last=True)

        def kind(pos, first, last):
            return (pos == 0 and not first) or pos == POS - 1, pos in (0, POS - 1), not (last and pos == POS - 1)

        block = ctx.enter_context(nc.Block())

        @block.sync
        def _(sp):
            def nat(t, n):
                rows = t[n:n + 1, :, :] if isinstance(n, int) else t[bass.ds(n, 1), :, :]
                return rows.rearrange("b (k p) d -> p (b k) d", p=P)

            def tail_rows(t, k, rs):
                return t[B - 1, :, :].rearrange("(k r q e) d -> k q r (e d)", k=KT, r=Q, e=2)[k][:, rs, :]

            def tail_tiles(k, rs):
                n = P // KT
                return x_in[k * n:(k + 1) * n, :, :].rearrange("q (r e) d -> q r (e d)", e=2)[:, rs, :]

            def load_adj(j):
                sp.dma_start(adj_row[j], adj[j * P:(j + 1) * P, :]).then_inc(s_adj[j], DMA)

            def load_x_in(n):
                sp.dma_start(x_in[:], nat(x, n)).then_inc(s_xin, DMA)

            def load_x_res(n):
                sp.dma_start(x_res[:], nat(x, n)).then_inc(s_xres, DMA)

            def exchange_to_nodes(done, n, moved):
                for c in range(CHUNKS):
                    sp.wait_ge(done, nth(n, c))
                    for r in (2 * c, 2 * c + 1):
                        for i in range(Q):
                            sp.dma_start(h_nodes[r * SQ:(r + 1) * SQ, i, :, :, :].rearrange("p a k d -> p (a k d)"),
                                         blocks[i * SQ:(i + 1) * SQ, r, :]).then_inc(moved, DMA)

            def exchange_to_features(i_h, done, n, moved):
                for half_ in range(2):
                    sp.wait_ge(done, nth(n, half_))
                    for i in (2 * half_, 2 * half_ + 1):
                        for r in range(Q):
                            sp.dma_start(hT[i_h][i * SQ:(i + 1) * SQ, r, :, :].rearrange("p a n -> p (a n)"),
                                         blocks[r * SQ:(r + 1) * SQ, i, :]).then_inc(moved, DMA)

            for j in range(KC):
                load_adj(j)
            load_x_in(0)
            for j in range(KC, KT):
                load_adj(j)
            for i, (w, src) in enumerate((("w3", w3_w), ("w4", w4_w), ("w5", w5_w))):
                sp.wait_ge(s_adjT, i + 1)
                sp.dma_start(w_row[w][:], src.rearrange("(a p) i -> p a i", p=P)).then_inc(s_w, DMA)
            sp.wait_ge(s_adjT, KC)
            for w, src in (("u3", u3_w), ("u5", u5_w)):
                sp.dma_start(w_row[w], src.rearrange("(a p) i -> p a i", p=P)).then_inc(s_w, DMA)
            exchange_to_features(0, s_blocks, 0, s_prep)
            sp.wait_ge(s_nat_lo, nth(0, 1))
            load_x_in(1)
            sp.wait_ge(s_adjT, KT)
            load_x_res(0)

            def turn(p, pos, first=False, last=False):
                g = POS * p + pos
                i = pos % 2
                final, fresh, prepare = kind(pos, first, last)
                n = 2 * p - 1 if pos == 0 else 2 * p
                if last and pos == 1:
                    sp.wait_ge(s_nat_lo, nth(g, 1))
                    for k in range(KT):
                        sp.dma_start(tail_tiles(k, slice(0, Q)), tail_rows(x, k, slice(0, Q))).then_inc(s_xin, DMA)
                if final:
                    exchange_to_nodes(s_fblocks, n, s_fin)
                if fresh and prepare:
                    exchange_to_features(1 - i, s_blocks, g + 1, s_prep)
                elif not fresh:
                    exchange_to_nodes(s_blocks, g + 1, s_prep)
                if pos == 1 and not last:
                    sp.wait_ge(s_nat_lo, nth(g, 1))
                    load_x_in(2 * p + 2)
                if pos == POS - 1 and not last:
                    sp.wait_ge(s_nat_lo, nth(g + 1, 1))
                    load_x_in(2 * p + 3)
                if final:
                    sp.wait_ge(s_out, n + 1)
                    sp.dma_start(nat(out, n), x_res[:]).then_inc(s_stored, DMA)
                    if not last:
                        sp.wait_ge(s_stored, DMA * (n + 1))
                        load_x_res(n + 1)

            turns(sp, turn)
            for c in range(CHUNKS):
                sp.wait_ge(s_out, B + c)
                rs = slice(2 * c, 2 * c + 2)
                for k in range(KT):
                    sp.dma_start(tail_rows(out, k, rs), tail_tiles(k, rs)).then_inc(s_stored, DMA)
            sp.wait_ge(s_stored, DMA * (B - 1 + CHUNKS * KT))

        @block.gpsimd
        def _(pool):
            nc.gpsimd.memset(ident[:], 0.0).then_inc(s_ident0, 1)
            nc.gpsimd.memset(minus_half[:], -0.5).then_inc(s_half, 1)
            pool.wait_ge(s_ident0, 1)
            nc.gpsimd.affine_select(out=ident[:], in_=ident[:], compare_op=ALU.not_equal, fill=1.0, base=0,
                                    pattern=[[-1, P]], channel_multiplier=1).then_inc(s_ident, 1)
            for i, b in enumerate((w3_b, u3_b, w4_b, w5_b, u5_b)):
                pool.dma_start(bias_row[i * DT:(i + 1) * DT, :], b.rearrange("(a p) -> a p", p=P)).then_inc(s_b, DMA)
            pool.wait_ge(s_half, 1)

            def rows(m, ks):
                pool.wait_ge(s_var, m + 1)
                nc.gpsimd.tensor_tensor(rstd[:, ks], var_eps[:, ks], minus_half[:, ks], ALU.pow).then_inc(s_rstd, 1)
                pool.wait_ge(s_mean, m + 1)
                pool.wait_ge(s_rstd, m + 1)
                nc.gpsimd.tensor_tensor(shift[:, ks], minus_mean[:, ks], rstd[:, ks], ALU.mult).then_inc(s_shift, 1)

            rows(0, slice(0, KT))
            with pool.Fori(1, B - 1) as n:
                pool.wait_ge(s_out, n)
                rows(n, slice(0, KT))
            pool.wait_ge(s_out, B - 1)
            for c in range(CHUNKS):
                rows(B - 1 + c, slice(c * TAIL, (c + 1) * TAIL))

        @block.tensor
        def _(pe):
            def product(ps, stationary, moving, opens=True, closes=True):
                for a in range(DT):
                    todo = [(s, m) for k, (m_hi, m_lo) in enumerate(moving)
                            for s, m in ((stationary(0, k, a), m_hi), (stationary(1, k, a), m_hi),
                                         (stationary(0, k, a), m_lo))]
                    for n, (s, m) in enumerate(todo):
                        last = nc.tensor.matmul(ps[:, a, :], s, m, start=opens and n == 0,
                                                stop=closes and n == len(todo) - 1)
                return last

            def weight(w):
                return lambda low, k, a: (w_hi[w], w_lo[w])[low][:, k, a * P:(a + 1) * P]

            def nodes(low, k, a):
                return (hnat_hi, hnat_lo)[low][:, k, a * P:(a + 1) * P]

            def halves(hi, lo):
                return [(hi[:, k, :], lo[:, k, :]) for k in range(DT)]

            def half_A(c, h):
                def cols(t):
                    return t.rearrange("p (r h n) -> p h r n", r=2, h=2)[:, h]
                for a in range(DT):
                    for k in range(KT):
                        for n, (stat, mov) in enumerate(((hnat_hi, adjT_hi), (hnat_lo, adjT_hi), (hnat_hi, adjT_lo))):
                            last = nc.tensor.matmul(cols(slot[c][:, a, :]), stat[:, k, a * P:(a + 1) * P],
                                                    cols(mov[:, k, c * CH:(c + 1) * CH]),
                                                    start=(k == 0 and n == 0), stop=(k == KT - 1 and n == 2))
                return last

            def adj_turn(j):
                pe.wait_ge(s_adj[j], DMA)
                if j >= 4:
                    pe.wait_ge(s_adj_lo, j - 1 if j >= 6 else 4)
                for k in range(KT):
                    last = nc.tensor.transpose(wide(adj_slot(j))[:, k * P:(k + 1) * P],
                                               adj_row[j][:, k * P:(k + 1) * P], ident[:])
                last.then_inc(s_adjT, 1)

            def weight_turn(s, ws):
                for i, w in enumerate(ws):
                    for it in range(DT):
                        for ot in range(DT):
                            last = nc.tensor.transpose(slot[s][:, i, it * D + ot * P:it * D + (ot + 1) * P],
                                                       w_row[w][:, ot, it * P:(it + 1) * P], ident[:])
                last.then_inc(s_wT, 1)

            pe.wait_ge(s_ident, 1)
            for j in range(KC):
                adj_turn(j)

            def weights_first():
                pe.wait_ge(s_w, 5 * DMA)
                pe.wait_ge(s_wsum, 3)
                weight_turn(2, ("u3", "w4"))
                weight_turn(3, ("w3", "w5"))

            def weights_last():
                pe.wait_ge(s_w_lo, 1)
                pe.wait_ge(s_b, 5 * DMA)
                nc.tensor.transpose(slot[2][:, 1, 0:5 * DT], bias_row[:], ident[0:5 * DT, 0:5 * DT])
                weight_turn(2, ("u5",))

            def turn(p, pos, first=False, last=False):
                g = POS * p + pos
                if first:
                    adj_turn(4)
                    adj_turn(5)
                pe.wait_ge(s_nat_lo, nth(g, 1))
                if first:
                    half_A(0, 0)
                    adj_turn(6)
                    adj_turn(7)
                    half_A(1, 0)
                    pe.wait_ge(s_adj_lo, KT)
                    weights_first()
                    half_A(0, 1).then_inc(s_A, 1)
                    weights_last()
                    half_A(1, 1).then_inc(s_A, 1)
                for c in range(CHUNKS if not first else 0):
                    pe.wait_ge(s_cand, nth(g - 1, c))
                    product(slot[c], nodes, [(adjT_hi[:, k, c * CH:(c + 1) * CH], adjT_lo[:, k, c * CH:(c + 1) * CH])
                                             for k in range(KT)]).then_inc(s_A, 1)
                for c in range(CHUNKS):
                    pe.wait_ge(s_h_lo, nth(g, c))
                    if first and c == 0:
                        pe.wait_ge(s_w_lo, 3)
                        pe.wait_ge(s_bias_in, 1)
                    elif c == 0:
                        pe.wait_ge(s_r_sum, nth(g - 1, 1))
                    else:
                        pe.wait_ge(s_agg_lo, nth(g, 1))
                    product(slot[2 - c], weight("u3"), halves(mov_hi[c], mov_lo[c])).then_inc(s_S, 1)
                    pe.wait_ge(s_agg_lo, nth(g, c))
                    if c == 1:
                        pe.wait_ge(s_S_cp, nth(g, 0))
                    elif not first:
                        pe.wait_ge(s_z_sum, nth(g - 1, 1))
                    product(slot[3 - c], weight("w4"), halves(agg_hi[c], agg_lo[c])).then_inc(s_R, 1)
                    if c == 1:
                        pe.wait_ge(s_r_sum, nth(g, 0))
                    product(slot[3 * c], weight("w3"), halves(agg_hi[c], agg_lo[c])).then_inc(s_Z, 1)
                for c in range(CHUNKS):
                    if c == 0:
                        pe.wait_ge(s_z_sum, nth(g, 0))
                    else:
                        pe.wait_ge(s_S_cp, nth(g, 1))
                    product(slot[c], weight("w5"), halves(agg_hi[c], agg_lo[c]), closes=False)
                    pe.wait_ge(s_rh_lo, nth(g, c))
                    product(slot[c], weight("u5"), halves(mov_hi[c], mov_lo[c]), opens=False).then_inc(s_V, 1)

            turns(pe, turn)
            g = POS * PAIRS - 1
            for c in range(CHUNKS):
                pe.wait_ge(s_h, nth(g, c))
                pe.wait_ge((s_r_sum, s_z_sum)[c], nth(g, 1))
                for t in range(TAIL):
                    r, e = 2 * c + t // 2, t % 2
                    for a in range(DT):
                        last = nc.tensor.transpose(wide(slot[2 + c])[:, t * D + a * P:t * D + (a + 1) * P],
                                                   hT[1][:, r, a, e::2], ident[:])
                last.then_inc(s_tail, 1)

        @block.scalar
        def _(act):
            def copy(dst, src):
                return nc.scalar.activation(dst, src, ACT.Copy)

            def normalise(m, t, tiles):
                act.wait_ge(s_shift, m + 1)
                for k in tiles:
                    row = nc.scalar.activation(t[:, k, :], t[:, k, :], ACT.Identity, scale=rstd[:, k:k + 1],
                                               bias=shift[:, k:k + 1])
                row.then_inc(s_out, 1)

            def adj_hi(j):
                act.wait_ge(s_adjT, j + 1)
                copy(*adj_columns(adjT_hi, j)).then_inc(s_adj_hi, 1)

            def weight_hi(s, n, ws):
                act.wait_ge(s_wT, n)
                for k, w in enumerate(ws):
                    last = copy(w_hi[w][:].rearrange("p a o -> p (a o)"), slot[s][:, k, :])
                last.then_inc(s_w_hi, 1)

            for j in range(KC):
                adj_hi(j)
            act.wait_ge(s_xin, DMA)
            for a in range(DT):
                copy(features(hnat_hi, a), features(x_in, a)).then_inc(s_nat_hi, 1)
            for j in range(KC, KT):
                adj_hi(j)
            weight_hi(2, 1, ("u3", "w4"))
            weight_hi(3, 2, ("w3", "w5"))

            def turn(p, pos, first=False, last=False):
                g = POS * p + pos
                final, fresh, prepare = kind(pos, first, last)
                for c in range(CHUNKS):
                    act.wait_ge(s_A, nth(g, c))
                    if not first:
                        act.wait_ge(s_V, nth(g - 1, c))
                    copy(agg_hi[c][:], slot[c][:]).then_inc(s_agg_hi, 1)
                    if first and c == 0:
                        weight_hi(2, 3, ("u5",))
                        copy(bias_in[:].rearrange("p b a -> p (b a)"), slot[2][:, 1, 0:5 * DT]).then_inc(s_bias_in, 1)
                if first:
                    act.wait_ge(s_bias, 3)
                for c in range(CHUNKS):
                    act.wait_ge(s_S, nth(g, c))
                    if not first:
                        act.wait_ge(s_step, nth(g - 1, c))
                    copy(zbuf[c][:], slot[2 - c][:]).then_inc(s_S_cp, 1)
                    act.wait_ge(s_r_sum, nth(g, c))
                    for a in range(DT):
                        r = nc.scalar.activation(rbuf[c][:, a, :], rbuf[c][:, a, :], ACT.Sigmoid,
                                                 bias=bias[:, 1, a:a + 1])
                    r.then_inc(s_r, 1)
                    act.wait_ge(s_rh, nth(g, c))
                    copy(mov_hi[c][:], rbuf[c][:]).then_inc(s_rh_hi, 1)
                    act.wait_ge(s_z_sum, nth(g, c))
                    for a in range(DT):
                        z = nc.scalar.activation(zbuf[c][:, a, :], zbuf[c][:, a, :], ACT.Sigmoid,
                                                 bias=bias[:, 0, a:a + 1])
                    z.then_inc(s_z, 1)
                if prepare:
                    act.wait_ge(s_A, nth(g, 1))
                    if fresh:
                        act.wait_ge(s_xin, DMA * (2 * p + (2 if pos == 0 else 3)))
                    else:
                        act.wait_ge(s_prep, EXCHANGE * (g + 2))
                    for a in range(DT):
                        copy(features(hnat_hi, a), features(x_in, a) if fresh else exchanged(a)).then_inc(s_nat_hi, 1)
                for c in range(CHUNKS):
                    act.wait_ge(s_V, nth(g, c))
                    for a in range(DT):
                        v = nc.scalar.activation(rbuf[c][:, a, :], slot[c][:, a, :], ACT.Tanh,
                                                 bias=bias[:, 2, a:a + 1])
                    v.then_inc(s_cand, 1)
                if final:
                    normalise(2 * p - 1 if pos == 0 else 2 * p, x_res, range(KT))

            turns(act, turn)
            for c in range(CHUNKS):
                normalise(B - 1 + c, x_in, range(c * TAIL, (c + 1) * TAIL))

        @block.vector
        def _(dve):
            def lo(dst, src, hi):
                return nc.vector.tensor_tensor(dst, src, hi.bitcast(F32), ALU.subtract)

            def adj_lo(j):
                dve.wait_ge(s_adj_hi, j + 1)
                (dst, src), (hi, _) = adj_columns(adjT_lo, j), adj_columns(adjT_hi, j)
                lo(dst, src, hi).then_inc(s_adj_lo, 1)

            def split_nodes(from_x, g):
                for a in range(DT):
                    dve.wait_ge(s_nat_hi, nth(g, a))
                    lo(features(hnat_lo, a), features(x_in, a) if from_x else exchanged(a),
                       features(hnat_hi, a)).then_inc(s_nat_lo, 1)

            def by_blocks(t):
                return t.rearrange("p (b d) -> p b d", d=SQ)

            def blocks_of_x(n):
                x_v = x_in[:].rearrange("p k (a i d) -> p i a k d", a=DT, i=Q)
                out_v = blocks[:].rearrange("p i (a k q) -> p i a k q", a=DT, k=KT)
                for i in range(Q):
                    t = nc.vector.transpose(out_v[:, i], x_v[:, i])
                    if i % 2:
                        t.then_inc(s_blocks, 1)

            def blocks_of_h(i, g, done):
                for c in range(CHUNKS):
                    dve.wait_ge(s_h, nth(g, c))
                    nc.vector.transpose(by_blocks(blocks[:, 2 * c:2 * c + 2, :].rearrange("p r n -> p (r n)")),
                                        by_blocks(hT[i][:, 2 * c:2 * c + 2, :, :].rearrange("p r a n -> p (r a n)"))
                                        ).then_inc(done, 1)

            for j in range(KC):
                adj_lo(j)
            split_nodes(True, 0)
            blocks_of_x(0)
            for j in (4, 5):
                adj_lo(j)
            dve.wait_ge(s_w, 5 * DMA)
            for w in ("w3", "w4", "w5"):
                nc.vector.tensor_tensor(w_row[w][:, :, 0:D], w_row[w][:, :, 0:D], w_row[w][:, :, D:2 * D],
                                        ALU.add).then_inc(s_wsum, 1)
            for j in (6, 7):
                adj_lo(j)

            def weight_lo(s, n, ws):
                dve.wait_ge(s_w_hi, n)
                for k, w in enumerate(ws):
                    last = lo(w_lo[w][:].rearrange("p a o -> p (a o)"), slot[s][:, k, :],
                              w_hi[w][:].rearrange("p a o -> p (a o)"))
                last.then_inc(s_w_lo, 1)

            weight_lo(2, 1, ("u3", "w4"))
            weight_lo(3, 2, ("w3", "w5"))

            def update(g, i, c):
                h, cand = chunk(i, c), like_h(rbuf[c])
                dve.wait_ge(s_cand, nth(g, c))
                nc.vector.tensor_tensor(cand, cand, h, ALU.subtract).then_inc(s_diff, 1)
                dve.wait_ge(s_z, nth(g, c))
                dve.wait_ge(s_diff, nth(g, c))
                nc.vector.tensor_tensor(rbuf[c][:], rbuf[c][:], zbuf[c][:], ALU.mult).then_inc(s_step, 1)
                dve.wait_ge(s_step, nth(g, c))
                nc.vector.tensor_tensor(h, h, cand, ALU.add).then_inc(s_h, 1)

            def residual(n, t):
                dve.wait_ge(s_fin, EXCHANGE * (n + 1))
                for a in range(DT):
                    nc.vector.tensor_tensor(features(t, a), features(t, a), exchanged(a), ALU.add).then_inc(s_res, 1)

            def variances(m, t, tiles, stats_before):
                if not isinstance(m, int) or m > 0:
                    dve.wait_ge(s_shift, m)
                for k in tiles:
                    nc.vector.bn_stats(stats[:, k, :], t[:, k, :]).then_inc(s_stat, 1)
                ks = slice(tiles[0], tiles[-1] + 1)
                dve.wait_ge(s_stat, stats_before + len(tiles))
                nc.vector.tensor_tensor(mean2[:, ks], stats[:, ks, 1], stats[:, ks, 4], ALU.add).then_inc(s_halves, 1)
                nc.vector.tensor_tensor(dev[:, ks], stats[:, ks, 1], stats[:, ks, 4], ALU.subtract).then_inc(s_halves, 1)
                nc.vector.tensor_tensor(sum_sq[:, ks], stats[:, ks, 2], stats[:, ks, 5], ALU.add).then_inc(s_halves, 1)
                dve.wait_ge(s_halves, 3 * m + 3)
                nc.vector.tensor_scalar(minus_mean[:, ks], mean2[:, ks], -0.5, None, ALU.mult).then_inc(s_mean, 1)
                nc.vector.scalar_tensor_tensor(sq_dev[:, ks], dev[:, ks], 0.25, dev[:, ks], ALU.mult,
                                               ALU.mult).then_inc(s_sq, 1)
                dve.wait_ge(s_sq, m + 1)
                nc.vector.scalar_tensor_tensor(var_eps[:, ks], sum_sq[:, ks], 1.0 / D, sq_dev[:, ks], ALU.mult,
                                               ALU.add).then_inc(s_var0, 1)
                dve.wait_ge(s_var0, m + 1)
                nc.vector.tensor_scalar(var_eps[:, ks], var_eps[:, ks], EPS, None, ALU.add).then_inc(s_var, 1)

            def turn(p, pos, first=False, last=False):
                g = POS * p + pos
                i = pos % 2
                final, fresh, prepare = kind(pos, first, last)
                n = 2 * p - 1 if pos == 0 else 2 * p
                if not first:
                    update(g - 1, 1 - i, 1)
                if final or not fresh:
                    dve.wait_ge(s_prep, EXCHANGE * (g + 1))
                    blocks_of_h(1 - i, g - 1, s_fblocks if final else s_blocks)
                for c in range(CHUNKS):
                    if pos in (0, 1):
                        dve.wait_ge(s_prep, EXCHANGE * (g + 1))
                    else:
                        dve.wait_ge(s_h, nth(g - 2, c))
                    if not first:
                        dve.wait_ge(s_V, nth(g - 1, c))
                    nc.vector.tensor_copy(like_h(mov_hi[c]), chunk(i, c)).then_inc(s_h_hi, 1)
                    dve.wait_ge(s_h_hi, nth(g, c))
                    lo(like_h(mov_lo[c]), chunk(i, c), like_h(mov_hi[c])).then_inc(s_h_lo, 1)
                for c in range(CHUNKS):
                    dve.wait_ge(s_agg_hi, nth(g, c))
                    lo(agg_lo[c][:], slot[c][:], agg_hi[c][:]).then_inc(s_agg_lo, 1)
                    if first and c == 0:
                        weight_lo(2, 3, ("u5",))
                        dve.wait_ge(s_bias_in, 1)
                        for k, (a, b) in enumerate(((0, 1), (2, 1), (3, 4))):
                            nc.vector.tensor_tensor(bias[:, k, :], bias_in[:, a, :], bias_in[:, b, :],
                                                    ALU.add).then_inc(s_bias, 1)
                if final:
                    dve.wait_ge(s_xres, DMA * (n + 1))
                    residual(n, x_res)
                    dve.wait_ge(s_res, nth(n, 1))
                    variances(n, x_res, range(KT), KT * n)
                for c in range(CHUNKS):
                    dve.wait_ge(s_R, nth(g, c))
                    dve.wait_ge(s_S_cp, nth(g, c))
                    nc.vector.tensor_tensor(rbuf[c][:], slot[3 - c][:], zbuf[c][:], ALU.add).then_inc(s_r_sum, 1)
                    dve.wait_ge(s_r, nth(g, c))
                    nc.vector.tensor_tensor(like_h(rbuf[c]), like_h(rbuf[c]), chunk(i, c), ALU.mult).then_inc(s_rh, 1)
                    dve.wait_ge(s_Z, nth(g, c))
                    nc.vector.tensor_tensor(zbuf[c][:], slot[3 * c][:], zbuf[c][:], ALU.add).then_inc(s_z_sum, 1)
                    dve.wait_ge(s_rh_hi, nth(g, c))
                    lo(mov_lo[c][:], rbuf[c][:], mov_hi[c][:]).then_inc(s_rh_lo, 1)
                    if c == 0 and fresh and prepare:
                        if final:
                            dve.wait_ge(s_fin, EXCHANGE * (n + 1))
                        else:
                            dve.wait_ge(s_prep, EXCHANGE * (g + 1))
                        dve.wait_ge(s_xin, DMA * (2 * p + (2 if pos == 0 else 3)))
                        blocks_of_x(g + 1)
                if prepare:
                    split_nodes(fresh, g + 1)
                update(g, i, 0)

            turns(dve, turn)
            update(POS * PAIRS - 1, 1, 1)
            dve.wait_ge(s_xin, DMA * (B + KT))
            for c in range(CHUNKS):
                rows = x_in[:, c * TAIL:(c + 1) * TAIL, :].rearrange("p k d -> p (k d)")
                dve.wait_ge(s_tail, c + 1)
                nc.vector.tensor_tensor(rows, rows, wide(slot[2 + c]), ALU.add).then_inc(s_res, 1)
                dve.wait_ge(s_res, DT * (B - 1) + c + 1)
                variances(B - 1 + c, x_in, range(c * TAIL, (c + 1) * TAIL), KT * (B - 1) + TAIL * c)


_INS = ["x", "adj"] + [f"L0_gnn_{n}" for n in ("w3_w", "w3_b", "u3_w", "u3_b", "w4_w", "w4_b", "w5_w", "w5_b", "u5_w", "u5_b")]


def kernel(**inputs):
    import numpy as _np
    import concourse.bacc as _bacc
    from concourse.bass_utils import run_bass_kernel_spmd as _run

    nc = _bacc.Bacc("TRN2", target_bir_lowering=False, num_devices=1)
    arrays, args = {}, []
    for name in _INS:
        a = _np.ascontiguousarray(inputs[name])
        arrays[f"in_{name}_dram"] = a
        args.append(nc.dram_tensor(f"in_{name}_dram", a.shape, mybir.dt.from_np(a.dtype), kind="ExternalInput").ap())
    args.append(nc.dram_tensor("out_dram", inputs["x"].shape, F32, kind="ExternalOutput").ap())
    gnn_program(nc, *args)
    return _run(nc, [arrays], core_ids=[0]).results[0]["out_dram"]
```
